# Optimizing a Trainium2 kernel written in Bass

```python
import numpy as np
import jax
import jax.numpy as jnp

def _softmax(x, axis=-1):
    return jax.nn.softmax(x, axis=axis)

def _gelu(x):
    return jax.nn.gelu(x, approximate=True)

def _silu(x):
    return jax.nn.silu(x)

def _sigmoid(x):
    return jax.nn.sigmoid(x)

def _layernorm(x, axis=-1, eps=1e-05):
    m = jnp.mean(x, axis=axis, keepdims=True)
    v = jnp.var(x, axis=axis, keepdims=True)
    return (x - m) / jnp.sqrt(v + eps)

def _scatter_add(tgt, idx, src, axis=0):
    return tgt.at[idx].add(src)

def _segment_sum(src, seg, n):
    return jax.ops.segment_sum(src, seg, n)
kernel_name = 'mk_dlrm_tower_d1_rec_r8_37bd3c'

def setup_inputs(seed: int=0):
    np.random.seed(seed)
    _w = jnp.asarray

    def _rec_inputs():
        import jax
        import jax.numpy as jnp
        _tk = jax.random.key(seed)
        dense_ctx = jax.random.normal(jax.random.fold_in(_tk, 190), (512, 16), jnp.float32)
        ids = jnp.stack([jax.random.randint(jax.random.fold_in(_tk, 200 + f), (512,), 0, v, jnp.int32) for f, v in enumerate([1250, 12500, 12500, 1250, 125000, 12500, 12500, 125000, 1250, 1000, 1250, 1000, 1250, 1250, 1250, 12500, 12500, 1250, 1250, 1250, 1000, 1000, 1250, 1250, 12500, 1000, 125000, 1250, 1000, 1250, 1250, 1250, 1250, 1000, 1250, 1250, 1000, 1000, 1000, 1000])], axis=1)
        tbl_0 = 0.05 * jax.random.normal(jax.random.fold_in(_tk, 500 + 0), (1250, 64), jnp.float32)
        tbl_1 = 0.05 * jax.random.normal(jax.random.fold_in(_tk, 500 + 1), (12500, 64), jnp.float32)
        tbl_2 = 0.05 * jax.random.normal(jax.random.fold_in(_tk, 500 + 2), (12500, 64), jnp.float32)
        tbl_3 = 0.05 * jax.random.normal(jax.random.fold_in(_tk, 500 + 3), (1250, 64), jnp.float32)
        tbl_4 = 0.05 * jax.random.normal(jax.random.fold_in(_tk, 500 + 4), (125000, 64), jnp.float32)
        tbl_5 = 0.05 * jax.random.normal(jax.random.fold_in(_tk, 500 + 5), (12500, 64), jnp.float32)
        tbl_6 = 0.05 * jax.random.normal(jax.random.fold_in(_tk, 500 + 6), (12500, 64), jnp.float32)
        tbl_7 = 0.05 * jax.random.normal(jax.random.fold_in(_tk, 500 + 7), (125000, 64), jnp.float32)
        tbl_8 = 0.05 * jax.random.normal(jax.random.fold_in(_tk, 500 + 8), (1250, 64), jnp.float32)
        tbl_9 = 0.05 * jax.random.normal(jax.random.fold_in(_tk, 500 + 9), (1000, 64), jnp.float32)
        tbl_10 = 0.05 * jax.random.normal(jax.random.fold_in(_tk, 500 + 10), (1250, 64), jnp.float32)
        tbl_11 = 0.05 * jax.random.normal(jax.random.fold_in(_tk, 500 + 11), (1000, 64), jnp.float32)
        tbl_12 = 0.05 * jax.random.normal(jax.random.fold_in(_tk, 500 + 12), (1250, 64), jnp.float32)
        tbl_13 = 0.05 * jax.random.normal(jax.random.fold_in(_tk, 500 + 13), (1250, 64), jnp.float32)
        tbl_14 = 0.05 * jax.random.normal(jax.random.fold_in(_tk, 500 + 14), (1250, 64), jnp.float32)
        tbl_15 = 0.05 * jax.random.normal(jax.random.fold_in(_tk, 500 + 15), (12500, 64), jnp.float32)
        tbl_16 = 0.05 * jax.random.normal(jax.random.fold_in(_tk, 500 + 16), (12500, 64), jnp.float32)
        tbl_17 = 0.05 * jax.random.normal(jax.random.fold_in(_tk, 500 + 17), (1250, 64), jnp.float32)
        tbl_18 = 0.05 * jax.random.normal(jax.random.fold_in(_tk, 500 + 18), (1250, 64), jnp.float32)
        tbl_19 = 0.05 * jax.random.normal(jax.random.fold_in(_tk, 500 + 19), (1250, 64), jnp.float32)
        tbl_20 = 0.05 * jax.random.normal(jax.random.fold_in(_tk, 500 + 20), (1000, 64), jnp.float32)
        tbl_21 = 0.05 * jax.random.normal(jax.random.fold_in(_tk, 500 + 21), (1000, 64), jnp.float32)
        tbl_22 = 0.05 * jax.random.normal(jax.random.fold_in(_tk, 500 + 22), (1250, 64), jnp.float32)
        tbl_23 = 0.05 * jax.random.normal(jax.random.fold_in(_tk, 500 + 23), (1250, 64), jnp.float32)
        tbl_24 = 0.05 * jax.random.normal(jax.random.fold_in(_tk, 500 + 24), (12500, 64), jnp.float32)
        tbl_25 = 0.05 * jax.random.normal(jax.random.fold_in(_tk, 500 + 25), (1000, 64), jnp.float32)
        tbl_26 = 0.05 * jax.random.normal(jax.random.fold_in(_tk, 500 + 26), (125000, 64), jnp.float32)
        tbl_27 = 0.05 * jax.random.normal(jax.random.fold_in(_tk, 500 + 27), (1250, 64), jnp.float32)
        tbl_28 = 0.05 * jax.random.normal(jax.random.fold_in(_tk, 500 + 28), (1000, 64), jnp.float32)
        tbl_29 = 0.05 * jax.random.normal(jax.random.fold_in(_tk, 500 + 29), (1250, 64), jnp.float32)
        tbl_30 = 0.05 * jax.random.normal(jax.random.fold_in(_tk, 500 + 30), (1250, 64), jnp.float32)
        tbl_31 = 0.05 * jax.random.normal(jax.random.fold_in(_tk, 500 + 31), (1250, 64), jnp.float32)
        tbl_32 = 0.05 * jax.random.normal(jax.random.fold_in(_tk, 500 + 32), (1250, 64), jnp.float32)
        tbl_33 = 0.05 * jax.random.normal(jax.random.fold_in(_tk, 500 + 33), (1000, 64), jnp.float32)
        tbl_34 = 0.05 * jax.random.normal(jax.random.fold_in(_tk, 500 + 34), (1250, 64), jnp.float32)
        tbl_35 = 0.05 * jax.random.normal(jax.random.fold_in(_tk, 500 + 35), (1250, 64), jnp.float32)
        tbl_36 = 0.05 * jax.random.normal(jax.random.fold_in(_tk, 500 + 36), (1000, 64), jnp.float32)
        tbl_37 = 0.05 * jax.random.normal(jax.random.fold_in(_tk, 500 + 37), (1000, 64), jnp.float32)
        tbl_38 = 0.05 * jax.random.normal(jax.random.fold_in(_tk, 500 + 38), (1000, 64), jnp.float32)
        tbl_39 = 0.05 * jax.random.normal(jax.random.fold_in(_tk, 500 + 39), (1000, 64), jnp.float32)
        _rk = jax.random.fold_in(_tk, 7)
        W_top1 = 0.0354441 * jax.random.normal(jax.random.fold_in(_tk, 801), (796, 512), jnp.float32)
        W_top2 = 0.0441942 * jax.random.normal(jax.random.fold_in(_tk, 802), (512, 256), jnp.float32)
        W_top3 = 0.0625 * jax.random.normal(jax.random.fold_in(_tk, 803), (256, 1), jnp.float32)
        b_top1 = jnp.zeros((512,), jnp.float32)
        b_top2 = jnp.zeros((256,), jnp.float32)
        return (dense_ctx, ids, tbl_0, tbl_1, tbl_2, tbl_3, tbl_4, tbl_5, tbl_6, tbl_7, tbl_8, tbl_9, tbl_10, tbl_11, tbl_12, tbl_13, tbl_14, tbl_15, tbl_16, tbl_17, tbl_18, tbl_19, tbl_20, tbl_21, tbl_22, tbl_23, tbl_24, tbl_25, tbl_26, tbl_27, tbl_28, tbl_29, tbl_30, tbl_31, tbl_32, tbl_33, tbl_34, tbl_35, tbl_36, tbl_37, tbl_38, tbl_39, W_top1, b_top1, W_top2, b_top2, W_top3)
    dense_ctx, ids, tbl_0, tbl_1, tbl_2, tbl_3, tbl_4, tbl_5, tbl_6, tbl_7, tbl_8, tbl_9, tbl_10, tbl_11, tbl_12, tbl_13, tbl_14, tbl_15, tbl_16, tbl_17, tbl_18, tbl_19, tbl_20, tbl_21, tbl_22, tbl_23, tbl_24, tbl_25, tbl_26, tbl_27, tbl_28, tbl_29, tbl_30, tbl_31, tbl_32, tbl_33, tbl_34, tbl_35, tbl_36, tbl_37, tbl_38, tbl_39, W_top1, b_top1, W_top2, b_top2, W_top3 = _rec_inputs()

    def _L0_rec_setup():
        import jax, jax.numpy as jnp
        import numpy as np
        B, N, E = (1024, 40, 64)
        P = N * (N - 1) // 2

        def _pair_indices(n):
            row, col = ([], [])
            for i in range(n - 1):
                for j in range(i + 1, n):
                    row.append(i)
                    col.append(j)
            return (np.asarray(row), np.asarray(col))
        key = jax.random.key(seed)
        k1, k2 = jax.random.split(key)
        inputs = jax.random.normal(k1, (B, N, E), dtype=jnp.float32)
        std = float(np.sqrt(2.0 / (E + E)))
        param = jax.random.normal(k2, (E, P, E), dtype=jnp.float32) * std
        return {'inputs': inputs, 'param': param}
    _L0_rec_all = _L0_rec_setup()
    _L0_rec_in = {k: v for k, v in _L0_rec_all.items() if k in ('param',)}
    del _L0_rec_all
    return {'dense_ctx': dense_ctx, 'ids': ids, 'tbl_0': tbl_0, 'tbl_1': tbl_1, 'tbl_2': tbl_2, 'tbl_3': tbl_3, 'tbl_4': tbl_4, 'tbl_5': tbl_5, 'tbl_6': tbl_6, 'tbl_7': tbl_7, 'tbl_8': tbl_8, 'tbl_9': tbl_9, 'tbl_10': tbl_10, 'tbl_11': tbl_11, 'tbl_12': tbl_12, 'tbl_13': tbl_13, 'tbl_14': tbl_14, 'tbl_15': tbl_15, 'tbl_16': tbl_16, 'tbl_17': tbl_17, 'tbl_18': tbl_18, 'tbl_19': tbl_19, 'tbl_20': tbl_20, 'tbl_21': tbl_21, 'tbl_22': tbl_22, 'tbl_23': tbl_23, 'tbl_24': tbl_24, 'tbl_25': tbl_25, 'tbl_26': tbl_26, 'tbl_27': tbl_27, 'tbl_28': tbl_28, 'tbl_29': tbl_29, 'tbl_30': tbl_30, 'tbl_31': tbl_31, 'tbl_32': tbl_32, 'tbl_33': tbl_33, 'tbl_34': tbl_34, 'tbl_35': tbl_35, 'tbl_36': tbl_36, 'tbl_37': tbl_37, 'tbl_38': tbl_38, 'tbl_39': tbl_39, 'W_top1': W_top1, 'b_top1': b_top1, 'W_top2': W_top2, 'b_top2': b_top2, 'W_top3': W_top3, 'L0_rec_param': _L0_rec_in['param']}

def reference(dense_ctx, ids, tbl_0, tbl_1, tbl_2, tbl_3, tbl_4, tbl_5, tbl_6, tbl_7, tbl_8, tbl_9, tbl_10, tbl_11, tbl_12, tbl_13, tbl_14, tbl_15, tbl_16, tbl_17, tbl_18, tbl_19, tbl_20, tbl_21, tbl_22, tbl_23, tbl_24, tbl_25, tbl_26, tbl_27, tbl_28, tbl_29, tbl_30, tbl_31, tbl_32, tbl_33, tbl_34, tbl_35, tbl_36, tbl_37, tbl_38, tbl_39, W_top1, b_top1, W_top2, b_top2, W_top3, L0_rec_param):
    import jax
    import jax.numpy as jnp

    def _L0_rec_ref(inputs, param):
        import jax, jax.numpy as jnp
        import numpy as np
        B, N, E = (1024, 40, 64)
        P = N * (N - 1) // 2

        def _pair_indices(n):
            row, col = ([], [])
            for i in range(n - 1):
                for j in range(i + 1, n):
                    row.append(i)
                    col.append(j)
            return (np.asarray(row), np.asarray(col))
        n = inputs.shape[1]
        rowidx, colidx = _pair_indices(n)
        p = inputs[:, rowidx]
        q = inputs[:, colidx]
        out = jnp.einsum('bie,fie,bif->bi', p, param, q)
        return out[:, None, :]
    e = jnp.stack([tbl_0[ids[:, 0]], tbl_1[ids[:, 1]], tbl_2[ids[:, 2]], tbl_3[ids[:, 3]], tbl_4[ids[:, 4]], tbl_5[ids[:, 5]], tbl_6[ids[:, 6]], tbl_7[ids[:, 7]], tbl_8[ids[:, 8]], tbl_9[ids[:, 9]], tbl_10[ids[:, 10]], tbl_11[ids[:, 11]], tbl_12[ids[:, 12]], tbl_13[ids[:, 13]], tbl_14[ids[:, 14]], tbl_15[ids[:, 15]], tbl_16[ids[:, 16]], tbl_17[ids[:, 17]], tbl_18[ids[:, 18]], tbl_19[ids[:, 19]], tbl_20[ids[:, 20]], tbl_21[ids[:, 21]], tbl_22[ids[:, 22]], tbl_23[ids[:, 23]], tbl_24[ids[:, 24]], tbl_25[ids[:, 25]], tbl_26[ids[:, 26]], tbl_27[ids[:, 27]], tbl_28[ids[:, 28]], tbl_29[ids[:, 29]], tbl_30[ids[:, 30]], tbl_31[ids[:, 31]], tbl_32[ids[:, 32]], tbl_33[ids[:, 33]], tbl_34[ids[:, 34]], tbl_35[ids[:, 35]], tbl_36[ids[:, 36]], tbl_37[ids[:, 37]], tbl_38[ids[:, 38]], tbl_39[ids[:, 39]]], axis=1)
    z = _L0_rec_ref(e, L0_rec_param)
    z = z.reshape(z.shape[0], -1)
    h = jnp.concatenate([z, dense_ctx], axis=1)
    h = jnp.maximum(h @ W_top1 + b_top1, 0.0)
    h = jnp.maximum(h @ W_top2 + b_top2, 0.0)
    y = h @ W_top3
    return y

_drawn_inputs = setup_inputs


def setup_inputs(seed=0):
    import zlib

    import numpy as np

    out = dict(_drawn_inputs(seed))
    spreads = {'b_top1': (0.0, 0.1), 'b_top2': (0.0, 0.1)}
    factors = {}
    for name, (base, spread) in spreads.items():
        noise = np.random.default_rng([zlib.crc32(name.encode()), seed]).standard_normal(out[name].shape)
        drawn = base * np.exp(spread * noise) if base else spread * noise
        out[name] = jnp.asarray(drawn.astype(out[name].dtype))
    for name, factor in factors.items():
        out[name] = (out[name] * factor).astype(out[name].dtype)
    return out
```

```python
import concourse.bass as bass
from concourse import mybir
from contextlib import ExitStack

F32 = mybir.dt.float32
U32 = mybir.dt.uint32
ALU = mybir.AluOpType
ACT = mybir.ActivationFunctionType
AX_X = mybir.AxisListType.X

P = 128
U_TILES = 3
SLABS = 3
X_SLOTS = 2
D_SLOTS = 2
A_SLOTS = 4
PAIRS = 8


def plan_units(N, E):
    def first_pair(i):
        return i * (N - 1) - i * (i - 1) // 2

    units = []
    busy = {"vector": 0.0, "scalar": 0.0}
    for k in range(N // 2 - 1, -1, -1):
        for i in (2 * k + 1, 2 * k):
            for j0 in range(i + 1, N, PAIRS):
                n = min(PAIRS, N - j0)
                for half in range(2):
                    busy["vector"] += 70 + 1.04 * 2 * n * E
                    cost = {"vector": 70 + 1.04 * 2 * n * E, "scalar": 2 * n * 220.0}
                    by = min(busy, key=lambda e: busy[e] + cost[e])
                    busy[by] += cost[by]
                    units.append({"k": k, "i": i, "j0": j0, "n": n, "half": half, "by": by,
                                  "pair": first_pair(i) + j0 - i - 1})
    return units


def pairwise_tower_kernel(nc, dense_ctx, ids, tables, param, W_top1, b_top1, W_top2, b_top2, W_top3, out):
    B, N = ids.shape
    E = tables[0].shape[1]
    BB = B // P
    NP = N * (N - 1) // 2
    DC = dense_ctx.shape[1]
    Z = NP + DC
    H1, H2 = W_top2.shape
    G = -(-Z // P)
    M1, M2 = H1 // P, H2 // P
    BANK = 512
    KS = N // 2
    LAST = G - 1
    assert BB == 4 and 2 * E == P and PAIRS * E == BANK and N % 2 == 0

    units = plan_units(N, E)
    NU = len(units)
    steps = [[u for u in range(NU) if units[u]["k"] == k] for k in range(KS)]

    def done_by(engine, u):
        return sum(1 for x in units[:u + 1] if x["by"] == engine)

    def group_units(g):
        lo, hi = g * P, min((g + 1) * P, NP)
        return max(u for u in range(NU) if units[u]["pair"] < hi and units[u]["pair"] + units[u]["n"] > lo)

    with ExitStack() as ctx:
        def sb(name, shape, dt=F32):
            return ctx.enter_context(nc.sbuf_tensor(name, shape, dt))

        def ps(name, shape):
            return ctx.enter_context(nc.psum_tensor(name, shape, F32))

        def sem(name):
            return ctx.enter_context(nc.semaphore(name))

        rows_id = sb("rows_id", [P, BB, N], ids.dtype)
        emb = sb("emb", [P, BB, N, E])
        xT = sb("xT", [P, X_SLOTS, B])
        slab = sb("slab", [P, SLABS, (N - 1) * E])
        prod_v = sb("prod_v", [P, D_SLOTS, 2 * BANK])
        prod_s = sb("prod_s", [P, A_SLOTS, 2 * BANK])
        z = sb("z", [P, BB, Z])
        zT = sb("zT", [P, G, B])
        w1 = sb("w1", [P, G, H1])
        w2 = sb("w2", [P, M1, H2])
        w3 = sb("w3", [P, M2])
        b1 = sb("b1", [P, M1])
        b2 = sb("b2", [P, M2])
        part = sb("part", [P, M1, B])
        h1 = sb("h1", [P, M1, B])
        h2 = sb("h2", [P, M2, B])
        yT = sb("yT", [1, B])
        ident = sb("ident", [P, P])

        upsum = [ps(f"upsum{t}", [P, 2, BANK]) for t in range(U_TILES)]
        tpsum = ps("tpsum", [P, B])
        mpsum = ps("mpsum", [P, B])

        ids_in = sem("ids_in")
        weights_in = sem("weights_in")
        dense_in = sem("dense_in")
        gathered = [sem(f"gathered{k}") for k in range(KS)]
        slab_in = [sem(f"slab_in{s}") for s in range(SLABS)]
        ident_zero = sem("ident_zero")
        ident_ready = sem("ident_ready")
        x_turned = sem("x_turned")
        x_ready = sem("x_ready")
        u_ready = sem("u_ready")
        multiplied = sem("multiplied")
        reduced_v = sem("reduced_v")
        reduced_s = sem("reduced_s")
        m_ready = sem("m_ready")
        m_taken = sem("m_taken")
        h1_ready = sem("h1_ready")
        sum_ready = sem("sum_ready")
        l1_done = sem("l1_done")
        l2_done = sem("l2_done")
        h2_ready = sem("h2_ready")
        y_done = sem("y_done")
        y_ready = sem("y_ready")
        stored = sem("stored")

        def step_before(k):
            return sum(len(steps[x]) for x in range(k + 1, KS))

        def group_rows(g):
            return min(P, Z - g * P)

        def slot(u):
            by = units[u]["by"]
            n = done_by(by, u) - 1
            ring = prod_v if by == "vector" else prod_s
            cols = 2 * units[u]["n"] * E
            return ring[:, n % (D_SLOTS if by == "vector" else A_SLOTS), 0:cols], n

        WEIGHTS = 16 * 6
        block = ctx.enter_context(nc.Block())

        @block.sync
        def _(sp):
            sp.dma_start(rows_id[:], ids.rearrange("(c p) f -> p c f", p=P)).then_inc(ids_in, 16)

            def load_slab(k):
                s = k % SLABS
                if k + SLABS < KS:
                    sp.wait_ge(u_ready, step_before(k + SLABS) + len(steps[k + SLABS]))
                for i in (2 * k, 2 * k + 1):
                    n = N - 1 - i
                    lo = (i % 2) * E
                    first = i * (N - 1) - i * (i - 1) // 2
                    if n:
                        sp.dma_start(slab[lo:lo + E, s, 0:n * E],
                                     param[:, first:first + n, :].rearrange("e q f -> e (q f)")).then_inc(slab_in[s], 16)

            for k in range(KS - 1, KS - 1 - SLABS, -1):
                load_slab(k)
            sp.dma_start(z[:, :, NP:Z], dense_ctx.rearrange("(c p) d -> p c d", p=P)).then_inc(dense_in, 16)
            sp.dma_start(w1[:, 0:LAST, :], W_top1[0:LAST * P, :].rearrange("(g p) n -> p g n", p=P)).then_inc(weights_in, 16)
            sp.dma_start(w1[0:group_rows(LAST), LAST, :], W_top1[LAST * P:Z, :]).then_inc(weights_in, 16)
            sp.dma_start(w2[:], W_top2.rearrange("(m p) n -> p m n", p=P)).then_inc(weights_in, 16)
            sp.dma_start(w3[:], W_top3).then_inc(weights_in, 16)
            sp.dma_start(b1[:], b_top1).then_inc(weights_in, 16)
            sp.dma_start(b2[:], b_top2).then_inc(weights_in, 16)
            for k in range(KS - 1 - SLABS, -1, -1):
                load_slab(k)
            sp.wait_ge(y_ready, 1)
            sp.dma_start(out.rearrange("b o -> o b"), yT[:]).then_inc(stored, 16)
            sp.wait_ge(stored, 16)

        @block.gpsimd
        def _(pool):
            pool.memset(ident[:], 0.0).then_inc(ident_zero, 1)
            pool.wait_ge(ident_zero, 1)
            pool.affine_select(out=ident[:], in_=ident[:], compare_op=ALU.not_equal, fill=1.0, base=0,
                               pattern=[[-1, P]], channel_multiplier=1).then_inc(ident_ready, 1)
            pool.wait_ge(ids_in, 16)
            for k in range(KS - 1, -1, -1):
                for f in (2 * k + 1, 2 * k):
                    for c in range(BB):
                        pool.indirect_dma_start(
                            emb[:, c, f, :], None, tables[f],
                            bass.IndirectOffsetOnAxis(ap=rows_id[:, c, f:f + 1].bitcast(U32), axis=0),
                        ).then_inc(gathered[k], 16)

        @block.tensor
        def _(pe):
            pe.wait_ge(ident_ready, 1)
            mm_count = [0]

            def turn_step(k):
                pe.wait_ge(gathered[k], 16 * 2 * BB)
                if k < KS - 1:
                    pe.wait_ge(x_ready, KS - 1 - k)
                for c in range(BB):
                    last = pe.transpose(tpsum[:, c * P:(c + 1) * P],
                                        emb[:, c, 2 * k:2 * k + 2, :].rearrange("p f e -> p (f e)"), ident[:])
                last.then_inc(x_turned, 1)

            def take_m():
                if mm_count[0]:
                    pe.wait_ge(m_taken, mm_count[0])
                mm_count[0] += 1

            def turn_group(g):
                u = group_units(g)
                if g == LAST:
                    pe.wait_ge(dense_in, 16)
                pe.wait_ge(reduced_v, done_by("vector", u))
                pe.wait_ge(reduced_s, done_by("scalar", u))
                take_m()
                for c in range(BB):
                    last = pe.transpose(mpsum[0:group_rows(g), c * P:(c + 1) * P],
                                        z[:, c, g * P:g * P + group_rows(g)], ident[:])
                last.then_inc(m_ready, 1)

            def layer1_part(m):
                if m == 0:
                    pe.wait_ge(weights_in, WEIGHTS)
                take_m()
                for g in range(LAST, 0, -1):
                    rows = group_rows(g)
                    last = pe.matmul(mpsum[:], w1[0:rows, g, m * P:(m + 1) * P], zT[0:rows, g, :],
                                     start=(g == LAST), stop=(g == 1))
                last.then_inc(m_ready, 1)

            after = {}
            for g in range(LAST, 0, -1):
                after.setdefault(min(group_units(g) + 8, NU - 1), []).append((turn_group, g))
            at = group_units(1) + 12
            for m in range(M1):
                after.setdefault(min(at + 3 * m, NU - 1), []).append((layer1_part, m))

            turn_step(KS - 1)
            for k in range(KS - 1, -1, -1):
                mine = steps[k]
                s, x = k % SLABS, k % X_SLOTS
                dmas = 1 if k == KS - 1 else 2
                before = sum(1 if q == KS - 1 else 2 for q in range(k + SLABS, KS, SLABS))
                pe.wait_ge(slab_in[s], 16 * (before + dmas))
                pe.wait_ge(x_ready, KS - k)
                turn_at = mine[max(0, len(mine) - 4)]
                for u in mine:
                    if u == turn_at and k > 0:
                        turn_step(k - 1)
                    d = units[u]
                    if u >= U_TILES:
                        pe.wait_ge(multiplied, u - U_TILES + 1)
                    lo = (d["i"] % 2) * E
                    c0 = (d["j0"] - d["i"] - 1) * E
                    for q in range(2):
                        c = 2 * d["half"] + q
                        last = pe.matmul(upsum[u % U_TILES][:, q, 0:d["n"] * E],
                                         xT[lo:lo + E, x, c * P:(c + 1) * P],
                                         slab[lo:lo + E, s, c0:c0 + d["n"] * E], start=True, stop=True)
                    last.then_inc(u_ready, 1)
                    for fn, arg in after.get(u, []):
                        fn(arg)

            turn_group(0)
            pe.wait_ge(m_taken, mm_count[0])
            pe.wait_ge(multiplied, NU)
            for m in range(M1):
                pe.matmul(upsum[m // 2][:, m % 2, :], w1[:, 0, m * P:(m + 1) * P], zT[:, 0, :],
                          start=True, stop=True).then_inc(l1_done, 1)
            for m in range(M1):
                pe.wait_ge(h1_ready, m + 1)
                for n in range(M2):
                    last = pe.matmul(upsum[2][:, n, :], w2[:, m, n * P:(n + 1) * P], h1[:, m, :],
                                     start=(m == 0), stop=(m == M1 - 1))
                    if m == M1 - 1:
                        last.then_inc(l2_done, 1)
            for n in range(M2):
                pe.wait_ge(h2_ready, n + 1)
                last = pe.matmul(mpsum[0:1, :], w3[:, n:n + 1], h2[:, n, :], start=(n == 0), stop=(n == M2 - 1))
            last.then_inc(y_done, 1)

        @block.vector
        def _(dve):
            pending = []

            def reduce(u):
                d = units[u]
                ring, n = slot(u)
                dve.wait_ge(multiplied, u + 1)
                c = 2 * d["half"]
                dve.tensor_reduce(z[:, c:c + 2, d["pair"]:d["pair"] + d["n"]],
                                  ring.rearrange("p (c q f) -> p c q f", c=2, f=E), AX_X, ALU.add).then_inc(reduced_v, 1)

            for u in range(NU):
                d = units[u]
                if u == 0 or units[u - 1]["k"] != d["k"]:
                    dve.wait_ge(gathered[d["k"]], 16 * 2 * BB)
                ring, n = slot(u)
                if d["by"] == "vector":
                    if n >= D_SLOTS:
                        dve.wait_ge(reduced_v, n - D_SLOTS + 1)
                elif n >= A_SLOTS:
                    dve.wait_ge(reduced_s, n - A_SLOTS + 1)
                dve.wait_ge(u_ready, u + 1)
                c = 2 * d["half"]
                w = d["n"] * E
                dve.tensor_tensor(ring.rearrange("p (c w) -> p c w", c=2), upsum[u % U_TILES][:, :, 0:w],
                                  emb[:, c:c + 2, d["j0"]:d["j0"] + d["n"], :].rearrange("p c j f -> p c (j f)"),
                                  ALU.mult).then_inc(multiplied, 1)
                if pending:
                    reduce(pending.pop(0))
                if d["by"] == "vector":
                    pending.append(u)
            for u in pending:
                reduce(u)
            for m in range(M1):
                dve.wait_ge(l1_done, m + 1)
                dve.wait_ge(m_taken, LAST + M1)
                dve.tensor_tensor(h1[:, m, :], upsum[m // 2][:, m % 2, :], part[:, m, :], ALU.add).then_inc(sum_ready, 1)

        @block.scalar
        def _(act):
            taken = [0]

            def copy_x(k):
                act.wait_ge(x_turned, KS - k)
                if k + X_SLOTS < KS:
                    act.wait_ge(u_ready, step_before(k + X_SLOTS) + len(steps[k + X_SLOTS]))
                act.activation(xT[:, k % X_SLOTS, :], tpsum[:], ACT.Copy).then_inc(x_ready, 1)

            def copy_group(g):
                taken[0] += 1
                act.wait_ge(m_ready, taken[0])
                rows = group_rows(g)
                act.activation(zT[0:rows, g, :], mpsum[0:rows, :], ACT.Copy).then_inc(m_taken, 1)

            def copy_part(m):
                taken[0] += 1
                act.wait_ge(m_ready, taken[0])
                if m == 0:
                    act.wait_ge(weights_in, WEIGHTS)
                act.activation(part[:, m, :], mpsum[:], ACT.Identity, bias=b1[:, m:m + 1]).then_inc(m_taken, 1)

            def reduce(u):
                d = units[u]
                ring, n = slot(u)
                act.wait_ge(multiplied, u + 1)
                for r in range(2):
                    for q in range(d["n"]):
                        at = (r * d["n"] + q) * E
                        last = act.activation(ring[:, at:at + E], ring[:, at:at + E], ACT.Copy,
                                              accum_out=z[:, 2 * d["half"] + r, d["pair"] + q:d["pair"] + q + 1])
                last.then_inc(reduced_s, 1)

            after = {}
            for g in range(LAST, 0, -1):
                after.setdefault(min(group_units(g) + 8, NU - 1), []).append((copy_group, g))
            at = group_units(1) + 12
            for m in range(M1):
                after.setdefault(min(at + 3 * m, NU - 1), []).append((copy_part, m))
            copy_x(KS - 1)
            late = []
            for k in range(KS - 1, -1, -1):
                mine = steps[k]
                turn_at = mine[max(0, len(mine) - 4)]
                for u in mine:
                    if u == turn_at and k > 0:
                        copy_x(k - 1)
                    for fn, arg in after.get(u, []):
                        late.append((fn, arg))
                    if units[u]["by"] == "scalar":
                        reduce(u)
                    while late:
                        fn, arg = late.pop(0)
                        fn(arg)
            copy_group(0)
            for m in range(M1):
                act.wait_ge(sum_ready, m + 1)
                act.activation(h1[:, m, :], h1[:, m, :], ACT.Relu).then_inc(h1_ready, 1)
            for n in range(M2):
                act.wait_ge(l2_done, n + 1)
                act.activation(h2[:, n, :], upsum[2][:, n, :], ACT.Relu, bias=b2[:, n:n + 1]).then_inc(h2_ready, 1)
            act.wait_ge(y_done, 1)
            act.activation(yT[:], mpsum[0:1, :], ACT.Copy).then_inc(y_ready, 1)


def kernel(**inputs):
    import numpy as np
    import concourse.bacc as bacc
    from concourse.bass_utils import run_bass_kernel_spmd

    nc = bacc.Bacc("TRN2", target_bir_lowering=False, num_devices=1)
    arrays = {}

    def give(name, a):
        a = np.ascontiguousarray(a)
        arrays[name] = a
        return nc.dram_tensor(name, a.shape, mybir.dt.from_np(a.dtype), kind="ExternalInput").ap()

    named = {n: give(n, inputs[n]) for n in ("dense_ctx", "ids", "W_top1", "W_top2")}
    for n in ("b_top1", "b_top2", "W_top3"):
        named[n] = give(n, np.asarray(inputs[n]).reshape(-1, P).T)
    n_fields = inputs["ids"].shape[1]
    tables = [give(f"tbl_{f}", inputs[f"tbl_{f}"]) for f in range(n_fields)]
    param = give("param", np.asarray(inputs["L0_rec_param"]).transpose(2, 1, 0))
    out = nc.dram_tensor("out", (inputs["ids"].shape[0], 1), F32, kind="ExternalOutput").ap()
    pairwise_tower_kernel(nc, tables=tables, param=param, out=out, **named)
    r = run_bass_kernel_spmd(nc, [arrays], core_ids=[0])
    return r.results[0]["out"]
```

```python
import concourse.bass as bass
from concourse import mybir
from contextlib import ExitStack

F32 = mybir.dt.float32
F32R = mybir.dt.float32r
U32 = mybir.dt.uint32
ALU = mybir.AluOpType
ACT = mybir.ActivationFunctionType
AX_X = mybir.AxisListType.X


P = 128
U_TILES = 3
X_SLOTS = 2
D_SLOTS = 5
D_LAG = 3
A_SLOTS = 4
PAIRS = 8
LOAD = 2 * PAIRS
E_SLOTS = 3
O_SLOTS = 4
AHEAD = 2
XH_BACK, XL_BACK, TURN_BACK = 20, 12, 10
POOL_SPLITS = 7
EVEN, ODD = 0, 1
POOL_GATHER = 1040
SLACK = 1000


def plan_units(N, E):
    def first_pair(i):
        return i * (N - 1) - i * (i - 1) // 2

    def on_vector(cols):
        return 70 + 1.04 * cols

    units, loads = [], []
    tensor = vector = scalar = 0.0
    pool = N * 4 * POOL_GATHER
    for k in range(N // 2 - 1, -1, -1):
        tensor = max(tensor, 12e3 + (N - 2 * k) * 4 * POOL_GATHER)
        for at, j in enumerate(range(2 * k + 1, N, PAIRS)):
            for half in range(2):
                for side in (EVEN, ODD):
                    i = 2 * k + side
                    j0 = max(j, i + 1)
                    n = min(j + PAIRS, N) - j0
                    if n <= 0:
                        continue
                    if side == EVEN and at % 2 == 0 and half == 0:
                        width = min(LOAD, N - j) * E
                        loads.append({"k": k, "j": j, "first": len(units)})
                        scalar += 100 + 0.83 * width
                        if k < POOL_SPLITS:
                            pool += 120 + 2.08 * width
                        else:
                            vector += on_vector(width)
                    if at == 0 and half == 0:
                        scalar += 1.5e3 / 2
                        vector += 340 / 2
                    cols = 2 * n * E
                    tensor += cols * (0.84 if side == EVEN else 1.67)
                    vector = max(vector, tensor) + on_vector(cols)
                    if scalar < vector + SLACK:
                        by = "scalar"
                        scalar = max(scalar, vector) + 2 * n * 240
                    elif k < POOL_SPLITS and pool < vector + SLACK:
                        by = "pool"
                        pool = max(pool, vector) + 120 + 1.04 * cols
                        vector += on_vector(cols // 2)
                    else:
                        by = "vector"
                        vector += on_vector(cols)
                    units.append({"k": k, "side": side, "i": i, "j0": j0, "n": n, "half": half, "by": by,
                                  "load": len(loads) - 1, "col": (j0 - loads[-1]["j"]) * E,
                                  "pair": first_pair(i) + j0 - i - 1})
    for w, load in enumerate(loads):
        load["end"] = (loads[w + 1]["first"] if w + 1 < len(loads) else len(units))
    return units, loads


def pairwise_tower_kernel(nc, dense_ctx, ids, tables, param, W_top1, b_top1, W_top2, b_top2, W_top3, out):
    B, N = ids.shape
    E = tables[0].shape[1]
    BB = B // P
    NP = N * (N - 1) // 2
    DC = dense_ctx.shape[1]
    Z = NP + DC
    H1, H2 = W_top2.shape
    G = -(-Z // P)
    M1, M2 = H1 // P, H2 // P
    BANK = 512
    KS = N // 2
    LAST = G - 1
    assert BB == 4 and 2 * E == P and PAIRS * E == BANK and N % 2 == 0

    units, loads = plan_units(N, E)
    NU, NL = len(units), len(loads)
    steps = [[u for u in range(NU) if units[u]["k"] == k] for k in range(KS)]

    def done_by(engine, u):
        names = ("vector", "pool") if engine == "vector" else (engine,)
        return sum(1 for x in units[:u + 1] if x["by"] in names)

    def group_end(g):
        lo, hi = g * P, min((g + 1) * P, NP)
        return max(u for u in range(NU) if units[u]["pair"] < hi and units[u]["pair"] + units[u]["n"] > lo)

    def group_rows(g):
        return min(P, Z - g * P)

    def units_through(k):
        return sum(len(steps[x]) for x in range(k, KS))

    def x_event(k, side):
        return 2 * (KS - 1 - k) + side

    def pool_splits(w):
        return loads[w]["k"] < POOL_SPLITS

    def splits_by(pool, w):
        return sum(1 for x in range(w + 1) if pool_splits(x) == pool)

    def load_width(w):
        return min(LOAD, N - loads[w]["j"]) * E

    def place(k, back):
        return steps[k][max(0, len(steps[k]) - back)]

    split_at = {}
    for w in range(AHEAD, NL):
        first, end = loads[w - AHEAD]["first"], loads[w - AHEAD]["end"]
        split_at.setdefault(("high", first), []).append(w)
        split_at.setdefault(("low", min(first + 3, end - 1)), []).append(w)
    tower_at = {}
    for g in range(LAST, 0, -1):
        tower_at.setdefault(min(group_end(g) + 9, NU - 1), []).append(("group", g))
    for m in range(M1):
        tower_at.setdefault(min(group_end(1) + 12 + 3 * m, NU - 1), []).append(("part", m))

    with ExitStack() as ctx:
        def sb(name, shape, dt=F32):
            return ctx.enter_context(nc.sbuf_tensor(name, shape, dt))

        def ps(name, shape):
            return ctx.enter_context(nc.psum_tensor(name, shape, F32))

        def sem(name):
            return ctx.enter_context(nc.semaphore(name))

        rows_id = sb("rows_id", [P, BB, N], ids.dtype)
        emb = sb("emb", [P, BB, N, E])
        x_parts = sb("x_parts", [P, BB, 2, E], F32R)
        xT_even = sb("xT_even", [P, X_SLOTS, B], F32R)
        xT_odd = sb("xT_odd", [P, X_SLOTS, B])
        w_raw = sb("w_raw", [P, E_SLOTS, LOAD * E])
        w_high = sb("w_high", [P, E_SLOTS, LOAD * E], F32R)
        w_low = sb("w_low", [P, E_SLOTS, LOAD * E], F32R)
        w_odd = sb("w_odd", [P, O_SLOTS, LOAD * E])
        prod_v = sb("prod_v", [P, D_SLOTS, 2 * BANK])
        prod_s = sb("prod_s", [P, A_SLOTS, 2 * BANK])
        z = sb("z", [P, BB, Z])
        zT = sb("zT", [P, G, B])
        w1 = sb("w1", [P, G, H1])
        w2 = sb("w2", [P, M1, H2])
        w3 = sb("w3", [P, M2])
        b1 = sb("b1", [P, M1])
        b2 = sb("b2", [P, M2])
        h1 = sb("h1", [P, M1, B])
        h2 = sb("h2", [P, M2, B])
        yT = sb("yT", [1, B])
        ident = sb("ident", [P, P])

        upsum = [ps(f"upsum{t}", [P, 2, BANK]) for t in range(U_TILES)]
        tpsum = ps("tpsum", [P, B])
        mpsum = ps("mpsum", [P, B])

        ids_in = sem("ids_in")
        weights_in = sem("weights_in")
        dense_in = sem("dense_in")
        gathered = [sem(f"gathered{k}") for k in range(KS)]
        raw_in = [sem(f"raw_in{s}") for s in range(E_SLOTS)]
        odd_in = [sem(f"odd_in{s}") for s in range(O_SLOTS)]
        ident_zero = sem("ident_zero")
        ident_ready = sem("ident_ready")
        zeroed = sem("zeroed")
        high_ready = sem("high_ready")
        low_by_v = sem("low_by_v")
        low_by_p = sem("low_by_p")
        xh_ready = sem("xh_ready")
        xl_ready = sem("xl_ready")
        x_turned = sem("x_turned")
        x_ready = sem("x_ready")
        u_ready = sem("u_ready")
        multiplied = sem("multiplied")
        halved = sem("halved")
        reduced_v = sem("reduced_v")
        reduced_s = sem("reduced_s")
        m_ready = sem("m_ready")
        m_taken = sem("m_taken")
        l1_done = sem("l1_done")
        h1_sum = sem("h1_sum")
        h1_ready = sem("h1_ready")
        l2_done = sem("l2_done")
        h2_ready = sem("h2_ready")
        y_done = sem("y_done")
        y_ready = sem("y_ready")
        stored = sem("stored")
        WEIGHTS = 16 * 6

        def slot(u):
            by = units[u]["by"]
            cols = 2 * units[u]["n"] * E
            if by == "scalar":
                n = done_by("scalar", u) - 1
                return prod_s[:, n % A_SLOTS, 0:cols], n
            n = done_by("vector", u) - 1
            return prod_v[:, n % D_SLOTS, 0:cols], n

        def wait_low(eng, w):
            eng.wait_ge(low_by_p if pool_splits(w) else low_by_v, splits_by(pool_splits(w), w))

        def make_low(eng, w, done):
            eng.wait_ge(high_ready, w + 1)
            s, width = w % E_SLOTS, load_width(w)
            eng.tensor_tensor(w_low[:, s, 0:width], w_raw[:, s, 0:width], w_high[:, s, 0:width].bitcast(F32),
                              ALU.subtract).then_inc(done, 1)

        block = ctx.enter_context(nc.Block())

        @block.sync
        def _(sp):
            sp.dma_start(rows_id[:], ids.rearrange("(c p) f -> p c f", p=P)).then_inc(ids_in, 16)

            def first_pair(i, j):
                return i * (N - 1) - i * (i - 1) // 2 + j - i - 1

            def load(w):
                k, j = loads[w]["k"], loads[w]["j"]
                n = load_width(w) // E
                if w >= E_SLOTS:
                    wait_low(sp, w - E_SLOTS)
                for lo in (0, E):
                    at = first_pair(2 * k, j)
                    sp.dma_start(w_raw[lo:lo + E, w % E_SLOTS, 0:n * E],
                                 param[:, at:at + n, :].rearrange("e q f -> e (q f)")).then_inc(raw_in[w % E_SLOTS], 16)
                if w == 0:
                    sp.wait_ge(zeroed, 2)
                if w >= O_SLOTS:
                    sp.wait_ge(u_ready, loads[w - O_SLOTS]["end"])
                at = first_pair(2 * k + 1, j)
                sp.dma_start(w_odd[E:P, w % O_SLOTS, 0:n * E],
                             param[:, at:at + n, :].rearrange("e q f -> e (q f)")).then_inc(odd_in[w % O_SLOTS], 16)

            for w in range(E_SLOTS):
                load(w)
            sp.dma_start(z[:, :, NP:Z], dense_ctx.rearrange("(c p) d -> p c d", p=P)).then_inc(dense_in, 16)
            sp.dma_start(w1[:, 0:LAST, :], W_top1[0:LAST * P, :].rearrange("(g p) n -> p g n", p=P)).then_inc(weights_in, 16)
            sp.dma_start(w1[0:group_rows(LAST), LAST, :], W_top1[LAST * P:Z, :]).then_inc(weights_in, 16)
            sp.dma_start(w2[:], W_top2.rearrange("(m p) n -> p m n", p=P)).then_inc(weights_in, 16)
            sp.dma_start(w3[:], W_top3).then_inc(weights_in, 16)
            sp.dma_start(b1[:], b_top1).then_inc(weights_in, 16)
            sp.dma_start(b2[:], b_top2).then_inc(weights_in, 16)
            for w in range(E_SLOTS, NL):
                load(w)
            sp.wait_ge(y_ready, 1)
            sp.dma_start(out.rearrange("b o -> o b"), yT[:]).then_inc(stored, 16)
            sp.wait_ge(stored, 16)

        @block.gpsimd
        def _(pool):
            pool.memset(ident[:], 0.0).then_inc(ident_zero, 1)
            pool.wait_ge(ident_zero, 1)
            pool.affine_select(out=ident[:], in_=ident[:], compare_op=ALU.not_equal, fill=1.0, base=0,
                               pattern=[[-1, P]], channel_multiplier=1).then_inc(ident_ready, 1)
            pool.wait_ge(ids_in, 16)
            for k in range(KS - 1, -1, -1):
                for f in (2 * k + 1, 2 * k):
                    for c in range(BB):
                        pool.indirect_dma_start(
                            emb[:, c, f, :], None, tables[f],
                            bass.IndirectOffsetOnAxis(ap=rows_id[:, c, f:f + 1].bitcast(U32), axis=0),
                        ).then_inc(gathered[k], 16)
            for u in range(NU):
                for w in split_at.get(("low", u), []):
                    if pool_splits(w):
                        make_low(pool, w, low_by_p)
                d = units[u]
                if d["by"] == "pool":
                    pool.wait_ge(multiplied, u + 1)
                    p = slot(u)[0].rearrange("p (q h f) -> p q h f", h=2, f=E // 2)
                    pool.tensor_tensor(p[:, :, 0, :], p[:, :, 0, :], p[:, :, 1, :], ALU.add).then_inc(halved, 1)

        @block.tensor
        def _(pe):
            pe.wait_ge(ident_ready, 1)
            results = [0]

            def turn(k, side):
                e = x_event(k, side)
                if e:
                    pe.wait_ge(x_ready, e)
                if side == EVEN:
                    pe.wait_ge(xl_ready, KS - k)
                else:
                    pe.wait_ge(gathered[k], 16 * 2 * BB)
                for c in range(BB):
                    if side == EVEN:
                        src = x_parts[:, c, :, :].rearrange("p h e -> p (h e)").bitcast(F32)
                    else:
                        src = emb[:, c, 2 * k:2 * k + 2, :].rearrange("p f e -> p (f e)")
                    last = pe.transpose(tpsum[:, c * P:(c + 1) * P], src, ident[:])
                last.then_inc(x_turned, 1)

            def take_mpsum():
                if results[0]:
                    pe.wait_ge(m_taken, results[0])
                results[0] += 1

            def turn_group(g):
                u = group_end(g)
                if g == LAST:
                    pe.wait_ge(dense_in, 16)
                pe.wait_ge(reduced_v, done_by("vector", u))
                pe.wait_ge(reduced_s, done_by("scalar", u))
                take_mpsum()
                for c in range(BB):
                    last = pe.transpose(mpsum[0:group_rows(g), c * P:(c + 1) * P],
                                        z[:, c, g * P:g * P + group_rows(g)], ident[:])
                last.then_inc(m_ready, 1)

            def layer1_part(m):
                if m == 0:
                    pe.wait_ge(weights_in, WEIGHTS)
                take_mpsum()
                for g in range(LAST, 0, -1):
                    rows = group_rows(g)
                    last = pe.matmul(mpsum[:], w1[0:rows, g, m * P:(m + 1) * P], zT[0:rows, g, :],
                                     start=(g == LAST), stop=(g == 1))
                last.then_inc(m_ready, 1)

            turn(KS - 1, EVEN)
            turn(KS - 1, ODD)
            for u in range(NU):
                d = units[u]
                k, w = d["k"], d["load"]
                if k > 0 and u == place(k, TURN_BACK):
                    turn(k - 1, EVEN)
                if k > 0 and u == place(k, TURN_BACK // 2):
                    turn(k - 1, ODD)
                if u == steps[k][0]:
                    pe.wait_ge(x_ready, x_event(k, ODD) + 1)
                if u == loads[w]["first"]:
                    wait_low(pe, w)
                    pe.wait_ge(odd_in[w % O_SLOTS], 16 * (w // O_SLOTS + 1))
                if u >= U_TILES:
                    pe.wait_ge(multiplied, u - U_TILES + 1)
                cols = slice(d["col"], d["col"] + d["n"] * E)
                for q in range(2):
                    c = 2 * d["half"] + q
                    tile = upsum[u % U_TILES][:, q, 0:d["n"] * E]
                    rows = slice(c * P, (c + 1) * P)
                    if d["side"] == EVEN:
                        pe.matmul(tile, xT_even[:, k % X_SLOTS, rows], w_high[:, w % E_SLOTS, cols], start=True, stop=False)
                        last = pe.matmul(tile, xT_even[:, k % X_SLOTS, rows], w_low[:, w % E_SLOTS, cols],
                                         start=False, stop=True)
                    else:
                        last = pe.matmul(tile, xT_odd[:, k % X_SLOTS, rows], w_odd[:, w % O_SLOTS, cols],
                                         start=True, stop=True)
                last.then_inc(u_ready, 1)
                for what, n in tower_at.get(u, []):
                    turn_group(n) if what == "group" else layer1_part(n)

            turn_group(0)
            pe.wait_ge(m_taken, results[0])
            pe.wait_ge(multiplied, NU)
            for m in range(M1):
                pe.matmul(upsum[m // 2][:, m % 2, :], w1[:, 0, m * P:(m + 1) * P], zT[:, 0, :],
                          start=True, stop=True).then_inc(l1_done, 1)
            for m in range(M1):
                pe.wait_ge(h1_ready, m + 1)
                for n in range(M2):
                    last = pe.matmul(upsum[2][:, n, :], w2[:, m, n * P:(n + 1) * P], h1[:, m, :],
                                     start=(m == 0), stop=(m == M1 - 1))
                    if m == M1 - 1:
                        last.then_inc(l2_done, 1)
            for n in range(M2):
                pe.wait_ge(h2_ready, n + 1)
                last = pe.matmul(mpsum[0:1, :], w3[:, n:n + 1], h2[:, n, :], start=(n == 0), stop=(n == M2 - 1))
            last.then_inc(y_done, 1)

        @block.vector
        def _(dve):
            dve.memset(w_odd[0:E, :, :], 0.0).then_inc(zeroed, 1)
            dve.memset(xT_odd[:], 0.0).then_inc(zeroed, 1)
            pending = []

            def reduce(u):
                d = units[u]
                ring, n = slot(u)
                c = 2 * d["half"]
                into = z[:, c:c + 2, d["pair"]:d["pair"] + d["n"]]
                if d["by"] == "pool":
                    dve.wait_ge(halved, sum(1 for x in units[:u + 1] if x["by"] == "pool"))
                    v = ring.rearrange("p (q h f) -> p q h f", h=2, f=E // 2)[:, :, 0, :]
                    v = v.rearrange("p (c q) f -> p c q f", c=2)
                else:
                    dve.wait_ge(multiplied, u + 1)
                    v = ring.rearrange("p (c q f) -> p c q f", c=2, f=E)
                dve.tensor_reduce(into, v, AX_X, ALU.add).then_inc(reduced_v, 1)

            def x_low(k):
                dve.wait_ge(gathered[k], 16 * 2 * BB)
                dve.wait_ge(xh_ready, KS - k)
                dve.tensor_tensor(x_parts[:, :, 1, :], emb[:, :, 2 * k, :], x_parts[:, :, 0, :].bitcast(F32),
                                  ALU.subtract).then_inc(xl_ready, 1)

            for w in range(AHEAD):
                make_low(dve, w, low_by_v)
            x_low(KS - 1)
            for u in range(NU):
                d = units[u]
                k = d["k"]
                if k > 0 and u == place(k, XL_BACK):
                    x_low(k - 1)
                for w in split_at.get(("low", u), []):
                    if not pool_splits(w):
                        make_low(dve, w, low_by_v)
                ring, n = slot(u)
                if d["by"] == "scalar":
                    if n >= A_SLOTS:
                        dve.wait_ge(reduced_s, n - A_SLOTS + 1)
                elif n >= D_SLOTS:
                    dve.wait_ge(reduced_v, n - D_SLOTS + 1)
                dve.wait_ge(u_ready, u + 1)
                c = 2 * d["half"]
                cols = d["n"] * E
                dve.tensor_tensor(ring.rearrange("p (c w) -> p c w", c=2), upsum[u % U_TILES][:, :, 0:cols],
                                  emb[:, c:c + 2, d["j0"]:d["j0"] + d["n"], :].rearrange("p c j f -> p c (j f)"),
                                  ALU.mult).then_inc(multiplied, 1)
                if d["by"] != "scalar":
                    pending.append(u)
                while pending and pending[0] <= u - D_LAG:
                    reduce(pending.pop(0))
            for u in pending:
                reduce(u)
            for m in range(M1):
                dve.wait_ge(l1_done, m + 1)
                if m == 0:
                    dve.wait_ge(m_taken, G + M1)
                dve.tensor_tensor(h1[:, m, :], upsum[m // 2][:, m % 2, :], h1[:, m, :], ALU.add).then_inc(h1_sum, 1)

        @block.scalar
        def _(act):
            taken = [0]

            def make_high(w):
                s, width = w % E_SLOTS, load_width(w)
                act.wait_ge(raw_in[s], 32 * (w // E_SLOTS + 1))
                if w >= E_SLOTS:
                    act.wait_ge(u_ready, loads[w - E_SLOTS]["end"])
                act.activation(w_high[:, s, 0:width], w_raw[:, s, 0:width], ACT.Copy).then_inc(high_ready, 1)

            def x_high(k):
                act.wait_ge(gathered[k], 16 * 2 * BB)
                if k < KS - 1:
                    act.wait_ge(x_turned, x_event(k + 1, EVEN) + 1)
                act.activation(x_parts[:, :, 0, :], emb[:, :, 2 * k, :], ACT.Copy).then_inc(xh_ready, 1)

            def copy_x(k, side):
                act.wait_ge(x_turned, x_event(k, side) + 1)
                if k + X_SLOTS < KS:
                    act.wait_ge(u_ready, units_through(k + X_SLOTS))
                if side == EVEN:
                    act.activation(xT_even[:, k % X_SLOTS, :], tpsum[:], ACT.Copy).then_inc(x_ready, 1)
                else:
                    act.activation(xT_odd[E:P, k % X_SLOTS, :], tpsum[E:P, :], ACT.Copy).then_inc(x_ready, 1)

            def copy_group(g):
                taken[0] += 1
                act.wait_ge(m_ready, taken[0])
                rows = group_rows(g)
                act.activation(zT[0:rows, g, :], mpsum[0:rows, :], ACT.Copy).then_inc(m_taken, 1)

            def copy_part(m):
                taken[0] += 1
                act.wait_ge(m_ready, taken[0])
                if m == 0:
                    act.wait_ge(weights_in, WEIGHTS)
                act.activation(h1[:, m, :], mpsum[:], ACT.Identity, bias=b1[:, m:m + 1]).then_inc(m_taken, 1)

            def reduce(u):
                d = units[u]
                ring = slot(u)[0]
                act.wait_ge(multiplied, u + 1)
                for r in range(2):
                    for q in range(d["n"]):
                        at = (r * d["n"] + q) * E
                        last = act.activation(ring[:, at:at + E], ring[:, at:at + E], ACT.Copy,
                                              accum_out=z[:, 2 * d["half"] + r, d["pair"] + q:d["pair"] + q + 1])
                last.then_inc(reduced_s, 1)

            for w in range(AHEAD):
                make_high(w)
            act.wait_ge(zeroed, 2)
            x_high(KS - 1)
            copy_x(KS - 1, EVEN)
            copy_x(KS - 1, ODD)
            for u in range(NU):
                k = units[u]["k"]
                if k > 0 and u == place(k, XH_BACK):
                    x_high(k - 1)
                for w in split_at.get(("high", u), []):
                    make_high(w)
                if k > 0 and u == place(k, TURN_BACK):
                    copy_x(k - 1, EVEN)
                if k > 0 and u == place(k, TURN_BACK // 2):
                    copy_x(k - 1, ODD)
                if units[u]["by"] == "scalar":
                    reduce(u)
                for what, n in tower_at.get(u, []):
                    copy_group(n) if what == "group" else copy_part(n)
            copy_group(0)
            for m in range(M1):
                act.wait_ge(h1_sum, m + 1)
                act.activation(h1[:, m, :], h1[:, m, :], ACT.Relu).then_inc(h1_ready, 1)
            for n in range(M2):
                act.wait_ge(l2_done, n + 1)
                act.activation(h2[:, n, :], upsum[2][:, n, :], ACT.Relu, bias=b2[:, n:n + 1]).then_inc(h2_ready, 1)
            act.wait_ge(y_done, 1)
            act.activation(yT[:], mpsum[0:1, :], ACT.Copy).then_inc(y_ready, 1)


def kernel(**inputs):
    import numpy as np
    import concourse.bacc as bacc
    from concourse.bass_utils import run_bass_kernel_spmd

    nc = bacc.Bacc("TRN2", target_bir_lowering=False, num_devices=1)
    arrays = {}

    def give(name, a):
        a = np.ascontiguousarray(a)
        arrays[name] = a
        return nc.dram_tensor(name, a.shape, mybir.dt.from_np(a.dtype), kind="ExternalInput").ap()

    named = {n: give(n, inputs[n]) for n in ("dense_ctx", "ids", "W_top1", "W_top2")}
    for n in ("b_top1", "b_top2", "W_top3"):
        named[n] = give(n, np.asarray(inputs[n]).reshape(-1, P).T)
    n_fields = inputs["ids"].shape[1]
    tables = [give(f"tbl_{f}", inputs[f"tbl_{f}"]) for f in range(n_fields)]
    param = give("param", np.asarray(inputs["L0_rec_param"]).transpose(2, 1, 0))
    out = nc.dram_tensor("out", (inputs["ids"].shape[0], 1), F32, kind="ExternalOutput").ap()
    pairwise_tower_kernel(nc, tables=tables, param=param, out=out, **named)
    r = run_bass_kernel_spmd(nc, [arrays], core_ids=[0])
    return r.results[0]["out"]
```

```python
import concourse.bass as bass
from concourse import mybir
from contextlib import ExitStack

F32 = mybir.dt.float32
F32R = mybir.dt.float32r
U32 = mybir.dt.uint32
ALU = mybir.AluOpType
ACT = mybir.ActivationFunctionType
AX_X = mybir.AxisListType.X


P = 128
PAIRS = 8
LOAD = 2 * PAIRS

U_TILES = 3
X_SLOTS = 4
R_SLOTS = 2
W_SLOTS = 4
D_SLOTS = 2
H_SLOTS = 4
A_SLOTS = 3

D_LAG = 4
H_LAG = 4
T_LAG = 2
SUM_GAP = 4
SUMS = 8
AHEAD = 2
LOW_AFTER = 4
XH_BACK, XL_BACK, TURN_BACK, COPY_BACK = 14, 9, 6, 6
EARLY_PART = 2
LATE_FIELDS = 20
TOWER_STEP = 2

SHARES = [(0, 0.4, 0.16, 0), (76, 0.31, 0.12, 0.4), (176, 0.34, 0, 0.45)]
LOW_BY_POOL = (65, 1.0)


def cut_units(N, E, BB):
    units, loads = [], []
    for i in range(N - 2, -1, -1):
        for j in range(i + 1, N, PAIRS):
            n = min(PAIRS, N - j)
            if (j - i - 1) % LOAD == 0:
                loads.append({"i": i, "j": j, "first": len(units), "width": min(LOAD, N - j) * E})
            blocks = BB if 2 * n <= PAIRS else BB // 2
            for c0 in range(0, BB, blocks):
                units.append({"i": i, "j0": j, "n": n, "c0": c0, "blocks": blocks, "cols": blocks * n * E,
                              "load": len(loads) - 1, "col": (j - loads[-1]["j"]) * E,
                              "pair": i * (N - 1) - i * (i - 1) // 2 + j - i - 1})
    for w, load in enumerate(loads):
        load["end"] = loads[w + 1]["first"] if w + 1 < len(loads) else len(units)
    return units, loads


def share_units(units, loads, E, busy):
    owed = {"scalar": 0.0, "pool": 0.0, "tensor": 0.0, "vector": 0.0}
    last_sum = -H_LAG
    for u, d in enumerate(units):
        now = [x for x in SHARES if x[0] <= u][-1]
        shares = dict(zip(("scalar", "tensor", "pool"), now[1:]))
        shares["vector"] = 1 - sum(shares.values())
        for by in owed:
            owed[by] += shares[by] * d["cols"]
        may = [by for by in owed if shares[by] > 0]
        free = (u - last_sum >= SUM_GAP and u + H_LAG < len(units)
                and all(b <= u + T_LAG or a >= u + H_LAG for a, b in busy))
        if "tensor" in may and not (free and d["cols"] == 2 * PAIRS * E):
            may.remove("tensor")
        d["by"] = max(may, key=lambda by: owed[by])
        owed[d["by"]] -= d["cols"]
        if d["by"] == "tensor":
            last_sum = u
    owed = 0.0
    for load in loads:
        load["low"] = "vector"
        if load["first"] >= LOW_BY_POOL[0]:
            owed += LOW_BY_POOL[1] * load["width"]
            if owed > 0:
                load["low"] = "pool"
                owed -= load["width"]


def pairwise_tower_kernel(nc, dense_ctx, ids, tables, param, W_top1, b_top1, W_top2, b_top2, W_top3, out):
    B, N = ids.shape
    E = tables[0].shape[1]
    BB = B // P
    NP = N * (N - 1) // 2
    DC = dense_ctx.shape[1]
    Z = NP + DC
    H1, H2 = W_top2.shape
    G = -(-Z // P)
    M1, M2 = H1 // P, H2 // P
    BANK = 512
    FIRST = N - 2
    LAST = G - 1
    STAGES = [(LAST, 2), (1, 1)]
    assert BB == 4 and 2 * E == P and PAIRS * E == BANK

    units, loads = cut_units(N, E, BB)
    NU, NL = len(units), len(loads)
    begins = [min(u for u in range(NU) if units[u]["i"] == i) for i in range(N - 1)]

    def done_by(engine, u):
        return sum(1 for x in units[:u + 1] if x["by"] == engine)

    def prepared(u):
        return done_by("pool", u) + done_by("tensor", u)

    def group_end(g):
        lo, hi = g * P, min((g + 1) * P, NP)
        return max(u for u in range(NU) if units[u]["pair"] < hi and units[u]["pair"] + units[u]["n"] > lo)

    def group_rows(g):
        return min(P, Z - g * P)

    def units_through(i):
        return begins[i - 1] if i else NU

    def pool_splits(w):
        return loads[w]["low"] == "pool"

    def splits_by(pool, w):
        return sum(1 for x in range(w + 1) if pool_splits(x) == pool)

    def preparations(back):
        at, unit = {}, 0
        for i in range(FIRST - 1, -1, -1):
            early = -(-back // EARLY_PART) if i > LATE_FIELDS else back
            unit = max(unit, begins[i] - early, begins[i + 2] if i + 2 <= FIRST else 0)
            at.setdefault(unit, []).append(i)
        return at

    high_at, low_at, turn_at, copy_at = [preparations(b) for b in (XH_BACK, XL_BACK, TURN_BACK, COPY_BACK)]

    split_at = {}
    for w in range(AHEAD, NL):
        first, end = loads[w - AHEAD]["first"], loads[w - AHEAD]["end"]
        split_at.setdefault(("high", first), []).append(w)
        split_at.setdefault(("low", min(first + LOW_AFTER, end - 1)), []).append(w)
    tower_at = {}
    busy = []
    free = 0
    for g in range(LAST, -1, -1):
        if g > 0:
            free = max(free, min(group_end(g) + 9, NU - 1))
            tower_at.setdefault(free, []).append(("group", g, 0))
            busy.append((free, free))
            free += 1
        for first, last in STAGES:
            if g == last:
                for m in range(M1):
                    busy.append((min(free + 1, NU - 1), min(free + 1 + (first - last) * TOWER_STEP, NU - 1)))
                    for x in range(first, last - 1, -1):
                        free = min(free + (1 if x == first else TOWER_STEP), NU - 1)
                        tower_at.setdefault(free, []).append(("product", m, x))
                    tower_at.setdefault(free, []).append(("part", m, first))
                free += 1

    share_units(units, loads, E, busy)
    sum_at = {u + T_LAG: u for u in range(NU) if units[u]["by"] == "tensor"}
    reduce_at = {}
    for by, lag, slots in ((("vector",), D_LAG, D_SLOTS), (("pool", "tensor"), H_LAG, H_SLOTS)):
        ring = [u for u in range(NU) if units[u]["by"] in by]
        for n, u in enumerate(ring):
            after = min(u + lag, ring[n + slots] - 1) if n + slots < len(ring) else u + lag
            reduce_at.setdefault(min(after, NU), []).append(u)

    with ExitStack() as ctx:
        def sb(name, shape, dt=F32):
            return ctx.enter_context(nc.sbuf_tensor(name, shape, dt))

        def ps(name, shape):
            return ctx.enter_context(nc.psum_tensor(name, shape, F32))

        def sem(name):
            return ctx.enter_context(nc.semaphore(name))

        rows_id = sb("rows_id", [P, BB, N], ids.dtype)
        emb = sb("emb", [P, BB, N, E])
        x_parts = sb("x_parts", [P, 2, BB, 2, E], F32R)
        xT = sb("xT", [P, X_SLOTS, B], F32R)
        w_raw = sb("w_raw", [P, R_SLOTS, LOAD * E])
        w_high = sb("w_high", [P, W_SLOTS, LOAD * E], F32R)
        w_low = sb("w_low", [P, W_SLOTS, LOAD * E], F32R)
        prod_v = sb("prod_v", [P, D_SLOTS, 2 * BANK])
        prod_h = sb("prod_h", [P, H_SLOTS, 2 * BANK])
        prod_s = sb("prod_s", [P, A_SLOTS, 2 * BANK])
        z = sb("z", [P, BB, Z])
        zT = sb("zT", [P, G, B])
        w1 = sb("w1", [P, G, H1])
        w2 = sb("w2", [P, M1, H2])
        w3 = sb("w3", [P, M2])
        b1 = sb("b1", [P, M1])
        b2 = sb("b2", [P, M2])
        h1 = sb("h1", [P, M1, B])
        h2 = sb("h2", [P, M2, B])
        yT = sb("yT", [1, B])
        ident = sb("ident", [P, P])

        upsum = [ps(f"upsum{t}", [P, 2, BANK]) for t in range(U_TILES)]
        tpsum = ps("tpsum", [P, B])
        mpsum = ps("mpsum", [P, B])

        ids_in = sem("ids_in")
        weights_in = sem("weights_in")
        dense_in = sem("dense_in")
        gathered = [sem(f"gathered{f}") for f in range(N)]
        raw_in = [sem(f"raw_in{s}") for s in range(R_SLOTS)]
        ident_zero = sem("ident_zero")
        ident_ready = sem("ident_ready")
        high_ready = sem("high_ready")
        low_by_v = sem("low_by_v")
        low_by_p = sem("low_by_p")
        xh_ready = sem("xh_ready")
        xl_ready = sem("xl_ready")
        x_turned = sem("x_turned")
        x_ready = sem("x_ready")
        u_ready = sem("u_ready")
        multiplied = sem("multiplied")
        halved = sem("halved")
        reduced_v = sem("reduced_v")
        summed = sem("summed")
        reduced_h = sem("reduced_h")
        reduced_s = sem("reduced_s")
        m_ready = sem("m_ready")
        m_taken = sem("m_taken")
        l1_done = sem("l1_done")
        h1_sum = sem("h1_sum")
        h1_ready = sem("h1_ready")
        l2_done = sem("l2_done")
        h2_ready = sem("h2_ready")
        y_done = sem("y_done")
        y_ready = sem("y_ready")
        stored = sem("stored")
        WEIGHTS = 16 * 6

        def slot(u):
            by = units[u]["by"]
            if by in ("pool", "tensor"):
                ring, slots, reduced, n = prod_h, H_SLOTS, reduced_h, prepared(u) - 1
            elif by == "vector":
                ring, slots, reduced, n = prod_v, D_SLOTS, reduced_v, done_by(by, u) - 1
            else:
                ring, slots, reduced, n = prod_s, A_SLOTS, reduced_s, done_by(by, u) - 1
            return ring[:, n % slots, 0:units[u]["blocks"] * units[u]["n"] * E], n, slots, reduced

        def u_tile(u):
            return upsum[u % U_TILES][:].rearrange("p q w -> p (q w)").rearrange("p (c w) -> p c w", c=units[u]["blocks"])

        def wait_low(eng, w):
            eng.wait_ge(low_by_p if pool_splits(w) else low_by_v, splits_by(pool_splits(w), w))

        def make_low(eng, w, done):
            eng.wait_ge(high_ready, w + 1)
            s, width = w % W_SLOTS, loads[w]["width"]
            eng.tensor_tensor(w_low[:, s, 0:width], w_raw[:, w % R_SLOTS, 0:width], w_high[:, s, 0:width].bitcast(F32),
                              ALU.subtract).then_inc(done, 1)

        def x_high(eng, i):
            eng.wait_ge(gathered[i], 16 * BB)
            if i + 2 <= FIRST:
                eng.wait_ge(x_turned, FIRST - i - 1)
            to, v = x_parts[:, i % 2, :, 0, :], emb[:, :, i, :]
            eng.tensor_copy(to, v).then_inc(xh_ready, 1)

        def copy_x(eng, i):
            eng.wait_ge(x_turned, FIRST - i + 1)
            if i + X_SLOTS <= FIRST:
                eng.wait_ge(u_ready, units_through(i + X_SLOTS))
            to = xT[:, i % X_SLOTS, :]
            eng.activation(to, tpsum[:], ACT.Copy).then_inc(x_ready, 1)

        block = ctx.enter_context(nc.Block())

        @block.sync
        def _(sp):
            sp.dma_start(rows_id[:], ids.rearrange("(c p) f -> p c f", p=P)).then_inc(ids_in, 16)

            def load(w):
                i, j, s = loads[w]["i"], loads[w]["j"], w % R_SLOTS
                n = loads[w]["width"] // E
                at = i * (N - 1) - i * (i - 1) // 2 + j - i - 1
                if w >= R_SLOTS:
                    wait_low(sp, w - R_SLOTS)
                for lo in (0, E):
                    sp.dma_start(w_raw[lo:lo + E, s, 0:n * E],
                                 param[:, at:at + n, :].rearrange("e q f -> e (q f)")).then_inc(raw_in[s], 16)

            for w in range(R_SLOTS):
                load(w)
            sp.dma_start(z[:, :, NP:Z], dense_ctx.rearrange("(c p) d -> p c d", p=P)).then_inc(dense_in, 16)
            sp.dma_start(w1[:, 0:LAST, :], W_top1[0:LAST * P, :].rearrange("(g p) n -> p g n", p=P)).then_inc(weights_in, 16)
            sp.dma_start(w1[0:group_rows(LAST), LAST, :], W_top1[LAST * P:Z, :]).then_inc(weights_in, 16)
            sp.dma_start(w2[:], W_top2.rearrange("(m p) n -> p m n", p=P)).then_inc(weights_in, 16)
            sp.dma_start(w3[:], W_top3).then_inc(weights_in, 16)
            sp.dma_start(b1[:], b_top1).then_inc(weights_in, 16)
            sp.dma_start(b2[:], b_top2).then_inc(weights_in, 16)
            for w in range(R_SLOTS, NL):
                load(w)
            sp.wait_ge(y_ready, 1)
            sp.dma_start(out.rearrange("b o -> o b"), yT[:]).then_inc(stored, 16)
            sp.wait_ge(stored, 16)

        @block.gpsimd
        def _(pool):
            pool.memset(ident[:], 0.0).then_inc(ident_zero, 1)
            pool.wait_ge(ident_zero, 1)
            pool.affine_select(out=ident[:], in_=ident[:], compare_op=ALU.not_equal, fill=1.0, base=0,
                               pattern=[[-1, P]], channel_multiplier=1).then_inc(ident_ready, 1)
            pool.wait_ge(ids_in, 16)
            for f in range(N - 1, -1, -1):
                for c in range(BB):
                    pool.indirect_dma_start(
                        emb[:, c, f, :], None, tables[f],
                        bass.IndirectOffsetOnAxis(ap=rows_id[:, c, f:f + 1].bitcast(U32), axis=0),
                    ).then_inc(gathered[f], 16)
            for u in range(NU):
                for w in split_at.get(("low", u), []):
                    if pool_splits(w):
                        make_low(pool, w, low_by_p)
                d = units[u]
                if d["by"] == "pool":
                    pool.wait_ge(multiplied, u + 1)
                    p = slot(u)[0].rearrange("p (q h f) -> p q h f", h=2, f=E // 2)
                    pool.tensor_tensor(p[:, :, 0, :], p[:, :, 0, :], p[:, :, 1, :], ALU.add).then_inc(halved, 1)

        @block.tensor
        def _(pe):
            pe.wait_ge(ident_ready, 1)
            results = [0]
            held_by = [None]

            def turn(i):
                pe.wait_ge(xl_ready, FIRST - i + 1)
                if i < FIRST:
                    pe.wait_ge(x_ready, FIRST - i)
                for c in range(BB):
                    last = pe.transpose(tpsum[:, c * P:(c + 1) * P],
                                        x_parts[:, i % 2, c, :, :].rearrange("p h e -> p (h e)").bitcast(F32), ident[:])
                last.then_inc(x_turned, 1)

            def take_mpsum(unit=None):
                if held_by[0] is not None:
                    pe.wait_ge(reduced_h, prepared(held_by[0]))
                elif results[0]:
                    pe.wait_ge(m_taken, results[0])
                held_by[0] = unit
                if unit is None:
                    results[0] += 1

            def sum_unit(u):
                pe.wait_ge(multiplied, u + 1)
                take_mpsum(u)
                v = slot(u)[0].rearrange("p (q k f) -> p k q f", k=SUMS, f=E // SUMS)
                to = mpsum[:, 0:units[u]["cols"] // SUMS].rearrange("p (q f) -> p q f", f=E // SUMS)
                for k in range(SUMS):
                    last = pe.matmul(to, ident[:], v[:, k, :, :], start=(k == 0), stop=(k == SUMS - 1))
                last.then_inc(summed, 1)

            def turn_group(g):
                u = group_end(g)
                if g == LAST:
                    pe.wait_ge(dense_in, 16)
                pe.wait_ge(reduced_v, done_by("vector", u))
                pe.wait_ge(reduced_h, prepared(u))
                pe.wait_ge(reduced_s, done_by("scalar", u))
                take_mpsum()
                for c in range(BB):
                    last = pe.transpose(mpsum[0:group_rows(g), c * P:(c + 1) * P],
                                        z[:, c, g * P:g * P + group_rows(g)], ident[:])
                last.then_inc(m_ready, 1)

            def layer1_product(m, g):
                first, last_g = [x for x in STAGES if x[0] >= g >= x[1]][0]
                if g == first:
                    pe.wait_ge(weights_in, WEIGHTS)
                    take_mpsum()
                rows = group_rows(g)
                last = pe.matmul(mpsum[:], w1[0:rows, g, m * P:(m + 1) * P], zT[0:rows, g, :],
                                 start=(g == first), stop=(g == last_g))
                if g == last_g:
                    last.then_inc(m_ready, 1)

            turn(FIRST)
            for u in range(NU):
                d = units[u]
                i, w = d["i"], d["load"]
                for x in turn_at.get(u, []):
                    turn(x)
                if u == begins[i]:
                    pe.wait_ge(x_ready, FIRST - i + 1)
                if u == loads[w]["first"]:
                    wait_low(pe, w)
                if u >= U_TILES:
                    pe.wait_ge(multiplied, u - U_TILES + 1)
                cols = slice(d["col"], d["col"] + d["n"] * E)
                tiles = u_tile(u)
                for q in range(d["blocks"]):
                    tile = tiles[:, q, 0:d["n"] * E]
                    x = xT[:, i % X_SLOTS, (d["c0"] + q) * P:(d["c0"] + q + 1) * P]
                    pe.matmul(tile, x, w_high[:, w % W_SLOTS, cols], start=True, stop=False)
                    last = pe.matmul(tile, x, w_low[:, w % W_SLOTS, cols], start=False, stop=True)
                last.then_inc(u_ready, 1)
                for what, n, g in tower_at.get(u, []):
                    if what == "group":
                        turn_group(n)
                    if what == "product":
                        layer1_product(n, g)
                if u in sum_at:
                    sum_unit(sum_at[u])

            turn_group(0)
            pe.wait_ge(m_taken, results[0])
            pe.wait_ge(multiplied, NU)
            for m in range(M1):
                pe.matmul(upsum[m // 2][:, m % 2, :], w1[:, 0, m * P:(m + 1) * P], zT[:, 0, :],
                          start=True, stop=True).then_inc(l1_done, 1)
            for m in range(M1):
                pe.wait_ge(h1_ready, m + 1)
                for n in range(M2):
                    last = pe.matmul(upsum[2][:, n, :], w2[:, m, n * P:(n + 1) * P], h1[:, m, :],
                                     start=(m == 0), stop=(m == M1 - 1))
                    if m == M1 - 1:
                        last.then_inc(l2_done, 1)
            for n in range(M2):
                pe.wait_ge(h2_ready, n + 1)
                last = pe.matmul(mpsum[0:1, :], w3[:, n:n + 1], h2[:, n, :], start=(n == 0), stop=(n == M2 - 1))
            last.then_inc(y_done, 1)

        @block.vector
        def _(dve):
            def reduce(u):
                d = units[u]
                ring, n, slots, reduced = slot(u)
                c, blocks = d["c0"], d["blocks"]
                into = z[:, c:c + blocks, d["pair"]:d["pair"] + d["n"]]
                if d["by"] == "pool":
                    dve.wait_ge(halved, done_by("pool", u))
                    v = ring.rearrange("p (q h f) -> p q h f", h=2, f=E // 2)[:, :, 0, :]
                    v = v.rearrange("p (c q) f -> p c q f", c=blocks)
                elif d["by"] == "tensor":
                    dve.wait_ge(summed, done_by("tensor", u))
                    v = mpsum[:, 0:d["cols"] // SUMS].rearrange("p (c q f) -> p c q f", c=blocks, f=E // SUMS)
                else:
                    dve.wait_ge(multiplied, u + 1)
                    v = ring.rearrange("p (c q f) -> p c q f", c=blocks, f=E)
                dve.tensor_reduce(into, v, AX_X, ALU.add).then_inc(reduced, 1)

            def x_low(i):
                dve.wait_ge(gathered[i], 16 * BB)
                dve.wait_ge(xh_ready, FIRST - i + 1)
                p = x_parts[:, i % 2, :, :, :]
                dve.tensor_tensor(p[:, :, 1, :], emb[:, :, i, :], p[:, :, 0, :].bitcast(F32),
                                  ALU.subtract).then_inc(xl_ready, 1)

            for w in range(AHEAD):
                make_low(dve, w, low_by_v)
            dve.wait_ge(gathered[N - 1], 16 * BB)
            x_high(dve, FIRST)
            x_low(FIRST)
            for u in range(NU):
                d = units[u]
                for x in high_at.get(u, []):
                    x_high(dve, x)
                for x in low_at.get(u, []):
                    x_low(x)
                for w in split_at.get(("low", u), []):
                    if not pool_splits(w):
                        make_low(dve, w, low_by_v)
                ring, n, slots, reduced = slot(u)
                if n >= slots:
                    dve.wait_ge(reduced, n - slots + 1)
                dve.wait_ge(u_ready, u + 1)
                c, blocks = d["c0"], d["blocks"]
                cols = d["n"] * E
                dve.tensor_tensor(ring.rearrange("p (c w) -> p c w", c=blocks), u_tile(u)[:, :, 0:cols],
                                  emb[:, c:c + blocks, d["j0"]:d["j0"] + d["n"], :].rearrange("p c j f -> p c (j f)"),
                                  ALU.mult).then_inc(multiplied, 1)
                for x in reduce_at.get(u, []):
                    reduce(x)
                for what, m, g in tower_at.get(u, []):
                    if what == "part" and g != LAST:
                        dve.wait_ge(m_ready, LAST + M1 + m + 1)
                        dve.tensor_tensor(h1[:, m, :], mpsum[:], h1[:, m, :], ALU.add).then_inc(m_taken, 1)
            for x in reduce_at.get(NU, []):
                reduce(x)
            for m in range(M1):
                dve.wait_ge(l1_done, m + 1)
                if m == 0:
                    dve.wait_ge(m_taken, LAST + 2 * M1)
                dve.tensor_tensor(h1[:, m, :], upsum[m // 2][:, m % 2, :], h1[:, m, :], ALU.add).then_inc(h1_sum, 1)

        @block.scalar
        def _(act):
            taken = [0]

            def make_high(w):
                s, width = w % W_SLOTS, loads[w]["width"]
                act.wait_ge(raw_in[w % R_SLOTS], 32 * (w // R_SLOTS + 1))
                if w >= W_SLOTS:
                    act.wait_ge(u_ready, loads[w - W_SLOTS]["end"])
                act.activation(w_high[:, s, 0:width], w_raw[:, w % R_SLOTS, 0:width], ACT.Copy).then_inc(high_ready, 1)

            def copy_group(g):
                taken[0] += 1
                act.wait_ge(m_ready, taken[0])
                rows = group_rows(g)
                act.activation(zT[0:rows, g, :], mpsum[0:rows, :], ACT.Copy).then_inc(m_taken, 1)

            def copy_part(m):
                taken[0] += 1
                act.wait_ge(m_ready, taken[0])
                if m == 0:
                    act.wait_ge(weights_in, WEIGHTS)
                act.activation(h1[:, m, :], mpsum[:], ACT.Identity, bias=b1[:, m:m + 1]).then_inc(m_taken, 1)

            def reduce(u):
                d = units[u]
                ring = slot(u)[0]
                act.wait_ge(multiplied, u + 1)
                for r in range(d["blocks"]):
                    for q in range(d["n"]):
                        at = (r * d["n"] + q) * E
                        last = act.activation(ring[:, at:at + E], ring[:, at:at + E], ACT.Copy,
                                              accum_out=z[:, d["c0"] + r, d["pair"] + q:d["pair"] + q + 1])
                last.then_inc(reduced_s, 1)

            for w in range(AHEAD):
                make_high(w)
            copy_x(act, FIRST)
            for u in range(NU):
                for w in split_at.get(("high", u), []):
                    make_high(w)
                for x in copy_at.get(u, []):
                    copy_x(act, x)
                if units[u]["by"] == "scalar":
                    reduce(u)
                for what, n, g in tower_at.get(u, []):
                    if what == "group":
                        copy_group(n)
                    if what == "part" and g == LAST:
                        copy_part(n)
                    if what == "part" and g != LAST:
                        taken[0] += 1
            copy_group(0)
            for m in range(M1):
                act.wait_ge(h1_sum, m + 1)
                act.activation(h1[:, m, :], h1[:, m, :], ACT.Relu).then_inc(h1_ready, 1)
            for n in range(M2):
                act.wait_ge(l2_done, n + 1)
                act.activation(h2[:, n, :], upsum[2][:, n, :], ACT.Relu, bias=b2[:, n:n + 1]).then_inc(h2_ready, 1)
            act.wait_ge(y_done, 1)
            act.activation(yT[:], mpsum[0:1, :], ACT.Copy).then_inc(y_ready, 1)


def kernel(**inputs):
    import numpy as np
    import concourse.bacc as bacc
    from concourse.bass_utils import run_bass_kernel_spmd

    nc = bacc.Bacc("TRN2", target_bir_lowering=False, num_devices=1)
    arrays = {}

    def give(name, a):
        a = np.ascontiguousarray(a)
        arrays[name] = a
        return nc.dram_tensor(name, a.shape, mybir.dt.from_np(a.dtype), kind="ExternalInput").ap()

    named = {n: give(n, inputs[n]) for n in ("dense_ctx", "ids", "W_top1", "W_top2")}
    for n in ("b_top1", "b_top2", "W_top3"):
        named[n] = give(n, np.asarray(inputs[n]).reshape(-1, P).T)
    n_fields = inputs["ids"].shape[1]
    tables = [give(f"tbl_{f}", inputs[f"tbl_{f}"]) for f in range(n_fields)]
    param = give("param", np.asarray(inputs["L0_rec_param"]).transpose(2, 1, 0))
    out = nc.dram_tensor("out", (inputs["ids"].shape[0], 1), F32, kind="ExternalOutput").ap()
    pairwise_tower_kernel(nc, tables=tables, param=param, out=out, **named)
    r = run_bass_kernel_spmd(nc, [arrays], core_ids=[0])
    return r.results[0]["out"]
```
